# Optimizing a Trainium2 kernel written in Bass

```python
import numpy as np
import jax
import jax.numpy as jnp

def _softmax(x, axis=-1):
    return jax.nn.softmax(x, axis=axis)

def _gelu(x):
    return jax.nn.gelu(x, approximate=True)

def _silu(x):
    return jax.nn.silu(x)

def _sigmoid(x):
    return jax.nn.sigmoid(x)

def _layernorm(x, axis=-1, eps=1e-05):
    m = jnp.mean(x, axis=axis, keepdims=True)
    v = jnp.var(x, axis=axis, keepdims=True)
    return (x - m) / jnp.sqrt(v + eps)

def _scatter_add(tgt, idx, src, axis=0):
    return tgt.at[idx].add(src)

def _segment_sum(src, seg, n):
    return jax.ops.segment_sum(src, seg, n)
kernel_name = 'mk_adj_resnorm_d1_adj_r2_9b4b28'

def setup_inputs(seed: int=0):
    np.random.seed(seed)
    _w = jnp.asarray

    def _rec_inputs():
        import jax
        import jax.numpy as jnp
        _gk = jax.random.key(seed)
        x = -0.0005207 + 1.001 * jax.random.normal(jax.random.fold_in(_gk, 1), (4096, 128), jnp.float32)
        _a = jax.random.bernoulli(jax.random.fold_in(_gk, 2), 0.000976562, (4096, 4096))
        _a = jnp.logical_or(_a, jnp.eye(4096, dtype=bool))
        _af = _a.astype(jnp.float32)
        _af = _af * jax.random.uniform(jax.random.fold_in(_gk, 3), (4096, 4096), jnp.float32, 0.05, 1)
        adj = _af
        return (x, adj)
    x, adj = _rec_inputs()

    def _L0_gnn_setup():
        import jax, jax.numpy as jnp
        import numpy as np
        N, IN_DIM, HID = (4096, 128, 128)

        def _gcn_layer(x, adj, W, b):
            d_inv_sqrt = (jnp.sum(adj, axis=1) + 1e-09) ** (-0.5)
            msg = d_inv_sqrt[:, None] * adj * d_inv_sqrt[None, :] @ x
            return jax.nn.relu(msg @ W + b)
        key = jax.random.key(seed)
        ks = jax.random.split(key, 9)
        feature_x = jax.random.normal(ks[0], (N, IN_DIM), dtype=jnp.float32)
        spatial_x = jax.random.normal(ks[1], (N, IN_DIM), dtype=jnp.float32)
        adj = jax.random.uniform(ks[2], (N, N), dtype=jnp.float32)
        s_in = 1.0 / np.sqrt(IN_DIM)
        s_hid = 1.0 / np.sqrt(2 * HID)
        W_f = jax.random.uniform(ks[3], (IN_DIM, HID), dtype=jnp.float32, minval=-s_in, maxval=s_in)
        b_f = jax.random.uniform(ks[4], (HID,), dtype=jnp.float32, minval=-s_in, maxval=s_in)
        W_s = jax.random.uniform(ks[5], (IN_DIM, HID), dtype=jnp.float32, minval=-s_in, maxval=s_in)
        b_s = jax.random.uniform(ks[6], (HID,), dtype=jnp.float32, minval=-s_in, maxval=s_in)
        W_att = jax.random.uniform(ks[7], (2 * HID, 1), dtype=jnp.float32, minval=-s_hid, maxval=s_hid)
        b_att = jax.random.uniform(ks[8], (1,), dtype=jnp.float32, minval=-s_hid, maxval=s_hid)
        return {'feature_x': feature_x, 'spatial_x': spatial_x, 'adj': adj, 'W_f': W_f, 'b_f': b_f, 'W_s': W_s, 'b_s': b_s, 'W_att': W_att, 'b_att': b_att}
    _L0_gnn_all = _L0_gnn_setup()
    _L0_gnn_in = {k: v for k, v in _L0_gnn_all.items() if k in ('spatial_x', 'W_f', 'b_f', 'W_s', 'b_s', 'W_att', 'b_att')}
    del _L0_gnn_all
    return {'x': x, 'adj': adj, 'L0_gnn_spatial_x': _L0_gnn_in['spatial_x'], 'L0_gnn_W_f': _L0_gnn_in['W_f'], 'L0_gnn_b_f': _L0_gnn_in['b_f'], 'L0_gnn_W_s': _L0_gnn_in['W_s'], 'L0_gnn_b_s': _L0_gnn_in['b_s'], 'L0_gnn_W_att': _L0_gnn_in['W_att'], 'L0_gnn_b_att': _L0_gnn_in['b_att']}

def reference(x, adj, L0_gnn_spatial_x, L0_gnn_W_f, L0_gnn_b_f, L0_gnn_W_s, L0_gnn_b_s, L0_gnn_W_att, L0_gnn_b_att):
    import jax
    import jax.numpy as jnp

    def _L0_gnn_ref(feature_x, spatial_x, adj, W_f, b_f, W_s, b_s, W_att, b_att):
        import jax, jax.numpy as jnp
        import numpy as np
        N, IN_DIM, HID = (4096, 128, 128)

        def _gcn_layer(x, adj, W, b):
            d_inv_sqrt = (jnp.sum(adj, axis=1) + 1e-09) ** (-0.5)
            msg = d_inv_sqrt[:, None] * adj * d_inv_sqrt[None, :] @ x
            return jax.nn.relu(msg @ W + b)
        H_f = _gcn_layer(feature_x, adj, W_f, b_f)
        H_s = _gcn_layer(spatial_x, adj, W_s, b_s)
        H_cat = jnp.concatenate([H_f, H_s], axis=1)
        attn = jax.nn.sigmoid(H_cat @ W_att + b_att)
        return attn * H_f + (1.0 - attn) * H_s
    x = _layernorm(x + _L0_gnn_ref(x, L0_gnn_spatial_x, adj, L0_gnn_W_f, L0_gnn_b_f, L0_gnn_W_s, L0_gnn_b_s, L0_gnn_W_att, L0_gnn_b_att), axis=-1)
    return x

_drawn_inputs = setup_inputs


def setup_inputs(seed=0):
    import zlib

    import numpy as np

    out = dict(_drawn_inputs(seed))
    spreads = {}
    factors = {'L0_gnn_b_f': 3.271, 'L0_gnn_b_s': 2.998, 'L0_gnn_W_att': 5.685}
    for name, (base, spread) in spreads.items():
        noise = np.random.default_rng([zlib.crc32(name.encode()), seed]).standard_normal(out[name].shape)
        drawn = base * np.exp(spread * noise) if base else spread * noise
        out[name] = jnp.asarray(drawn.astype(out[name].dtype))
    for name, factor in factors.items():
        out[name] = (out[name] * factor).astype(out[name].dtype)
    return out
```

```python
from contextlib import ExitStack

import concourse.bass as bass
from concourse import mybir

ALU = mybir.AluOpType
ACT = mybir.ActivationFunctionType
AX = mybir.AxisListType
F32 = mybir.dt.float32
F32R = mybir.dt.float32r
BF16 = mybir.dt.bfloat16

P = 128
Q = 4
B = P // Q
UNIT = 8
SLOTS = 3
SPLITS = 3
XB = 4
LEAD = 4
OUT_ROWS = 4
AHEAD = 10


def build(nc, x, adj, sx, W_f, b_f, W_s, b_s, W_att, b_att, out):
    N, F = x.shape
    H = W_f.shape[1]
    H2 = 2 * H
    T = N // P
    CB = N // Q
    assert F == P and H == P and T == CB // B

    late = []
    for a in range(T // 2):
        late += [a] if a == T - 2 - a else [a, T - 2 - a]
    late = late[:T - 1]
    loads = [(1, r) for r in range(T)] + [(2, r) for r in late]

    units, first_unit, last_unit = [], [], []
    for n, (p, r) in enumerate(loads):
        first_unit.append(len(units))
        lo, hi = (0, r + 1) if p == 1 else (r + 1, T)
        while lo < hi:
            m = min(UNIT - lo % UNIT, hi - lo)
            units.append((n, r, lo, m))
            lo += m
        last_unit.append(len(units) - 1)
    row_units = [range(first_unit[n], last_unit[n] + 1) for n in range(len(loads))]

    def xw_at(r):
        return [t for t in (2 * r + LEAD, 2 * r + LEAD + 1) if t < T]

    def degrees_with(r):
        return ([r] if r <= AHEAD else []) + ([r + 1] if AHEAD <= r < T - 1 else [])

    def due(k, lag):
        return [n for n in range(len(loads)) if last_unit[n] + lag == k]

    def finished(k, lag):
        return [n - (T - 1) for n in due(k, lag) if n >= T - 1]

    L_SUM, L_RELU, L_GATE, L_STATS, L_NORM = 1, 2, 3, 4, 5

    adj_v = adj.rearrange("(c r x) (q y) -> r q x c y", c=Q, x=B, q=Q)
    x_v = x.rearrange("(c r x) f -> c x r f", c=Q, x=B)
    sx_v = sx.rearrange("(c r x) f -> c x r f", c=Q, x=B)
    out_v = out.rearrange("(c r x) f -> c x r f", c=Q, x=B)
    bf_v = b_f.rearrange("(a h) -> a h", a=1).to_broadcast([P, H])
    bs_v = b_s.rearrange("(a h) -> a h", a=1).to_broadcast([P, H])
    watt_v = W_att.rearrange("h a -> a h").to_broadcast([P, H2])
    batt_v = b_att.rearrange("(a h) -> a h", a=1).to_broadcast([P, 1])

    with ExitStack() as ctx:
        def sb(name, shape, dt=F32):
            return ctx.enter_context(nc.sbuf_tensor(name, shape, dt))

        def ps(name, shape, dt=F32):
            return ctx.enter_context(nc.psum_tensor(name, shape, dt))

        def sem(name):
            return ctx.enter_context(nc.semaphore(name))

        Y = sb("Y", [P, T, 2 * H2], F32R)
        part = sb("part", [P, T, H2])
        xres = sb("xres", [P, T, F])
        sxs = sb("sxs", [P, 2, XB, F])
        raw = sb("raw", [P, SLOTS, Q, CB])
        Ah = sb("Ah", [P, SPLITS, UNIT * P], F32R)
        Al = sb("Al", [P, SPLITS, UNIT * P], F32R)
        xT = sb("xT", [P, 2, 2 * P])
        junk = sb("junk", [P, CB], BF16)
        rs = sb("rs", [P, T, Q])
        degw = sb("degw", [P, P])
        degs = sb("degs", [P, T])
        D = sb("D", [P, T])
        ident = sb("ident", [P, P])
        same_x = sb("same_x", [P, P])
        ones = sb("ones", [P, 1])
        mhalf = sb("mhalf", [P, 1])
        epsc = sb("epsc", [P, 1])
        Wfs = sb("Wfs", [P, H2])
        bias = sb("bias", [P, H2])
        watt = sb("watt", [P, H2])
        batt = sb("batt", [P, 1])
        sums = sb("sums", [P, 2 * H2])
        hh = sb("hh", [P, H2])
        hr = sb("hr", [P, H2])
        hw = sb("hw", [P, H2])
        lg = sb("lg", [P, 2])
        dif = sb("dif", [P, F])
        xs = sb("xs", [P, F])
        yv = sb("yv", [P, 2, F])
        st6 = sb("st6", [P, 6])
        mv = sb("mv", [P, 2, 4])

        turned = ps("turned", [P, 2, UNIT * P])
        acc = ps("acc", [P, 2, 2 * H2])
        ps_x = ps("ps_x", [P, 4 * P])
        ps_y = ps("ps_y", [P, 4 * P])

        raw_in = [sem(f"raw_in{i}") for i in range(SLOTS)]
        raw_in_g = [sem(f"raw_in_g{i}") for i in range(SLOTS)]
        feat_in = [sem(f"feat_in{i}") for i in range(2)]
        const_in = sem("const_in")
        pool_const = sem("pool_const")
        pool_step = sem("pool_step")
        turned_ok = sem("turned_ok")
        high_ok = sem("high_ok")
        low_ok = sem("low_ok")
        used = sem("used")
        rs_act = sem("rs_act")
        rs_dve = sem("rs_dve")
        degw_ok = sem("degw_ok")
        deg_ok = sem("deg_ok")
        degs_ok = sem("degs_ok")
        D_ok = sem("D_ok")
        Yh_ok = sem("Yh_ok")
        Yl_ok = sem("Yl_ok")
        xT_ps = sem("xT_ps")
        xT_ok = sem("xT_ok")
        xw_ps = sem("xw_ps")
        xw_ok = sem("xw_ok")
        part_ok = sem("part_ok")
        base_ok = sem("base_ok")
        half_ok = sem("half_ok")
        sums_ok = sem("sums_ok")
        hsum_ok = sem("hsum_ok")
        h_ok = sem("h_ok")
        relu_ok = sem("relu_ok")
        hw_ok = sem("hw_ok")
        logit_ok = sem("logit_ok")
        gate_ok = sem("gate_ok")
        dif_ok = sem("dif_ok")
        xs_ok = sem("xs_ok")
        gated_ok = sem("gated_ok")
        y_ok = sem("y_ok")
        stats_ok = sem("stats_ok")
        aggr_ok = sem("aggr_ok")
        vare_ok = sem("vare_ok")
        rstd_ok = sem("rstd_ok")
        norm_ok = sem("norm_ok")
        stored = sem("stored")

        block = ctx.enter_context(nc.Block())

        def raw_free(eng, n):
            if n < SLOTS:
                return
            p, r = loads[n - SLOTS]
            eng.wait_ge(turned_ok, last_unit[n - SLOTS] + 1)
            if p == 1:
                eng.wait_ge(rs_act, (Q - 1) * (r + 1))
                eng.wait_ge(rs_dve, r + 1)

        def quadrants(n):
            return ((0, 1), (2, 3)) if n < T else (range(Q), ())

        def load_raw(eng, n, mine, arrived):
            p, r = loads[n]
            y0 = 0 if p == 1 else B * (r + 1)
            for q in mine:
                eng.dma_start(raw[B * q:B * (q + 1), n % SLOTS, :, y0:CB],
                              adj_v[r, q, :, :, y0:CB]).then_inc(arrived[n % SLOTS], 16)

        def raw_here(eng, n):
            same_slot = range(n % SLOTS, n + 1, SLOTS)
            eng.wait_ge(raw_in[n % SLOTS], 16 * sum(len(quadrants(i)[0]) for i in same_slot))
            eng.wait_ge(raw_in_g[n % SLOTS], 16 * sum(len(quadrants(i)[1]) for i in same_slot))

        def load_features(eng, m):
            if m >= 2:
                eng.wait_ge(xT_ps, XB * (m - 1))
            for c in range(Q):
                eng.dma_start(xres[B * c:B * (c + 1), XB * m:XB * (m + 1), :],
                              x_v[c, :, XB * m:XB * (m + 1), :]).then_inc(feat_in[m % 2], 16)
                eng.dma_start(sxs[B * c:B * (c + 1), m % 2, :, :],
                              sx_v[c, :, XB * m:XB * (m + 1), :]).then_inc(feat_in[m % 2], 16)

        stores, done = [], set()
        for j in range(T):
            r = loads[T - 1 + j][1]
            done.add(r)
            a = OUT_ROWS * (r // OUT_ROWS)
            if done >= set(range(a, a + OUT_ROWS)):
                stores.append((j + 1, a))

        @block.sync
        def _(sp):
            sp.dma_start(Wfs[:, 0:H], W_f).then_inc(const_in, 16)
            sp.dma_start(Wfs[:, H:H2], W_s).then_inc(const_in, 16)
            load_features(sp, 0)
            load_raw(sp, 0, quadrants(0)[0], raw_in)
            sp.dma_start(bias[:, 0:H], bf_v).then_inc(const_in, 16)
            sp.dma_start(bias[:, H:H2], bs_v).then_inc(const_in, 16)
            sp.dma_start(watt[:, :], watt_v).then_inc(const_in, 16)
            sp.dma_start(batt[:, :], batt_v).then_inc(const_in, 16)
            load_features(sp, 1)
            for n in range(1, len(loads)):
                raw_free(sp, n)
                load_raw(sp, n, quadrants(n)[0], raw_in)
                if n % 2 == 0 and n // 2 + 1 < T // XB:
                    load_features(sp, n // 2 + 1)
            for j, a in stores:
                sp.wait_ge(norm_ok, j)
                for c in range(Q):
                    sp.dma_start(out_v[c, :, a:a + OUT_ROWS, :],
                                 part[B * c:B * (c + 1), a:a + OUT_ROWS, 0:F]).then_inc(stored, 16)
            sp.wait_ge(stored, 16 * Q * len(stores))

        @block.tensor
        def _(pe):
            def xw(t, degrees):
                m = t // XB
                pe.wait_ge(feat_in[m % 2], 32 * Q * (m // 2 + 1))
                if t >= 1:
                    pe.wait_ge(xT_ok, t)
                if degrees:
                    pe.wait_ge(degs_ok, degrees)
                pe.transpose(ps_x[:, 0:P], xres[:, t, :], ident[:, :])
                pe.transpose(ps_x[:, P:2 * P], sxs[:, m % 2, t % XB, :], ident[:, :]).then_inc(xT_ps, 1)
                pe.wait_ge(xT_ok, t + 1)
                if t >= 1:
                    pe.wait_ge(xw_ok, t)
                pe.matmul(ps_y[:, 0:H], xT[:, t % 2, 0:P], Wfs[:, 0:H], start=True, stop=True)
                pe.matmul(ps_y[:, H:H2], xT[:, t % 2, P:2 * P], Wfs[:, H:H2],
                          start=True, stop=True).then_inc(xw_ps, 1)

            def degree(r):
                pe.wait_ge(degw_ok, r + 1)
                if r >= 1:
                    pe.wait_ge(degs_ok, r)
                pe.matmul(ps_x[:, 2 * P:2 * P + 1], degw[:, :], ones[:, :],
                          start=True, stop=True).then_inc(deg_ok, 1)

            def multiply(k, first, last):
                n, _, lo, m = units[k]
                pe.wait_ge(low_ok, k + 1)
                for i in range(m):
                    t = lo + i
                    pe.matmul(acc[:, n % 2, :], Ah[:, k % SPLITS, i * P:(i + 1) * P], Y[:, t, :],
                              start=(first and i == 0), stop=False)
                    mm = pe.matmul(acc[:, n % 2, 0:H2], Al[:, k % SPLITS, i * P:(i + 1) * P],
                                   Y[:, t, 0:H2], start=False, stop=(last and i == m - 1))
                mm.then_inc(used, 1)

            pe.wait_ge(pool_const, 1)
            pe.wait_ge(const_in, 16 * 6)
            for t in range(LEAD):
                xw(t, 0)
            for n, (p, r) in enumerate(loads):
                if p == 1:
                    for t in xw_at(r):
                        xw(t, r)
                if 2 <= n < T + 1:
                    pe.wait_ge(part_ok, n - 1)
                elif n >= T + 1:
                    pe.wait_ge(sums_ok, n - T)
                for k in row_units[n]:
                    if p == 1 and k == last_unit[n]:
                        for d in degrees_with(r):
                            degree(d)
                        pe.wait_ge(Yl_ok, r + 1)
                    multiply(k, k == first_unit[n], k == last_unit[n])

        @block.vector
        def _(dve):
            def turn(k):
                n, r, lo, m = units[k]
                if k == first_unit[n]:
                    raw_here(dve, n)
                if k >= 2:
                    dve.wait_ge(high_ok, k - 1)
                    dve.wait_ge(low_ok, k - 1)
                src = raw[:, n % SLOTS, :, lo * B:(lo + m) * B].rearrange("p c (t y) -> p t c y", y=B)
                dst = turned[:, k % 2, 0:m * P].rearrange("p (t c x) -> p t c x", c=Q, x=B)
                dve.transpose(dst, src).then_inc(turned_ok, 1)

            def low(k):
                m = units[k][3]
                dve.wait_ge(high_ok, k + 1)
                if k >= SPLITS:
                    dve.wait_ge(used, k - SPLITS + 1)
                dve.tensor_tensor(Al[:, k % SPLITS, 0:m * P], turned[:, k % 2, 0:m * P],
                                  Ah[:, k % SPLITS, 0:m * P], ALU.subtract).then_inc(low_ok, 1)

            def row_sum(r):
                raw_here(dve, r)
                dve.tensor_reduce(rs[:, r, Q - 1:Q], raw[:, r % SLOTS, Q - 1, :], AX.X,
                                  ALU.add).then_inc(rs_dve, 1)

            def xw_out(t):
                dve.wait_ge(xw_ps, t + 1)
                dve.tensor_copy(part[:, t, :], ps_y[:, 0:H2]).then_inc(xw_ok, 1)

            def scale_y(r):
                dve.wait_ge(deg_ok, r + 1)
                dve.tensor_scalar(degs[:, r:r + 1], ps_x[:, 2 * P:2 * P + 1], 1e-9, None,
                                  ALU.add).then_inc(degs_ok, 1)
                dve.wait_ge(D_ok, r + 1)
                dve.wait_ge(xw_ok, r + 1)
                dve.tensor_scalar(Y[:, r, 0:H2], part[:, r, :], D[:, r:r + 1], None,
                                  ALU.mult).then_inc(Yh_ok, 1)
                dve.wait_ge(Yh_ok, r + 1)
                dve.scalar_tensor_tensor(out=Y[:, r, H2:2 * H2], in0=part[:, r, :], scalar=D[:, r:r + 1],
                                         in1=Y[:, r, 0:H2], op0=ALU.mult,
                                         op1=ALU.subtract).then_inc(Yl_ok, 1)

            def store_part(n):
                dve.wait_ge(used, last_unit[n] + 1)
                dve.wait_ge(Yl_ok, n + 1)
                dve.tensor_reduce(part[:, n, :], acc[:, n % 2, :].rearrange("p (a h) -> p h a", a=2), AX.X,
                                  ALU.add).then_inc(part_ok, 1)

            def stats(j):
                dve.wait_ge(y_ok, j + 1)
                if j >= 1:
                    dve.wait_ge(aggr_ok, j)
                dve.bn_stats(st6[:, :], yv[:, j % 2, :]).then_inc(stats_ok, 1)
                dve.wait_ge(stats_ok, j + 1)
                if j >= 2:
                    dve.wait_ge(norm_ok, j - 1)
                dve.bn_aggr(mv[:, j % 2, 0:2], st6[:, :]).then_inc(aggr_ok, 1)

            def normalise(j):
                r = loads[T - 1 + j][1]
                dve.wait_ge(rstd_ok, j + 1)
                dve.tensor_scalar(part[:, r, 0:F], yv[:, j % 2, :], mv[:, j % 2, 0:1], mv[:, j % 2, 3:4],
                                  ALU.subtract, ALU.mult).then_inc(norm_ok, 1)

            def beside(k):
                for n in due(k, L_SUM):
                    if n < T - 1:
                        store_part(n)
                for j in finished(k, L_NORM):
                    normalise(j)
                for j in finished(k, L_STATS):
                    stats(j)

            for t in range(LEAD):
                xw_out(t)
            for k, (n, r, lo, m) in enumerate(units):
                p = loads[n][0]
                turn(k)
                if p == 1 and k == first_unit[n] and r <= AHEAD:
                    row_sum(r)
                if k >= 1:
                    low(k - 1)
                    beside(k - 1)
                if p == 1 and k == first_unit[n]:
                    for t in xw_at(r):
                        xw_out(t)
                if p == 1 and k == last_unit[n]:
                    if AHEAD <= r < T - 1:
                        row_sum(r + 1)
                    scale_y(r)
            low(len(units) - 1)
            for k in range(len(units) - 1, len(units) + L_NORM):
                beside(k)

        @block.scalar
        def _(act):
            junk_writes = [0, 0]

            def junk_free():
                if junk_writes[0]:
                    act.wait_ge(rs_act, junk_writes[0])
                if junk_writes[1]:
                    act.wait_ge(logit_ok, junk_writes[1])

            def high(k):
                m = units[k][3]
                act.wait_ge(turned_ok, k + 1)
                if k >= SPLITS:
                    act.wait_ge(used, k - SPLITS + 1)
                act.activation(Ah[:, k % SPLITS, 0:m * P], turned[:, k % 2, 0:m * P],
                               ACT.Copy).then_inc(high_ok, 1)

            def row_sum(r, c):
                raw_here(act, r)
                junk_free()
                junk_writes[0] += 1
                act.activation(junk[:, 0:CB], raw[:, r % SLOTS, c, :], ACT.Copy,
                               accum_out=rs[:, r, c:c + 1]).then_inc(rs_act, 1)

            def xT_out(t):
                act.wait_ge(xT_ps, t + 1)
                if t >= 2:
                    act.wait_ge(xw_ps, t - 1)
                act.activation(xT[:, t % 2, :], ps_x[:, 0:2 * P], ACT.Copy).then_inc(xT_ok, 1)

            def evacuate(j):
                n = T - 1 + j
                r = loads[n][1]
                act.wait_ge(used, last_unit[n] + 1)
                act.wait_ge(D_ok, r + 1)
                if j >= 1:
                    act.wait_ge(hsum_ok, j)
                act.activation(sums[:, :], acc[:, n % 2, :], ACT.Copy,
                               scale=D[:, r:r + 1]).then_inc(sums_ok, 1)

            def relu(j):
                act.wait_ge(h_ok, j + 1)
                if j >= 1:
                    act.wait_ge(xs_ok, j)
                act.activation(hr[:, :], hh[:, :], ACT.Relu).then_inc(relu_ok, 1)

            def gate(j):
                act.wait_ge(hw_ok, j + 1)
                if j >= 1:
                    act.wait_ge(gate_ok, j)
                junk_free()
                junk_writes[1] += 1
                act.activation(junk[:, 0:H2], hw[:, :], ACT.Copy,
                               accum_out=lg[:, 0:1]).then_inc(logit_ok, 1)
                act.wait_ge(logit_ok, j + 1)
                if j >= 1:
                    act.wait_ge(gated_ok, j)
                act.activation(lg[:, 1:2], lg[:, 0:1], ACT.Sigmoid, bias=batt[:, :]).then_inc(gate_ok, 1)

            def beside(k):
                for j in finished(k, L_GATE):
                    gate(j)
                for j in finished(k, L_RELU):
                    relu(j)
                for j in finished(k, L_SUM):
                    evacuate(j)

            for t in range(LEAD):
                xT_out(t)
            act.wait_ge(const_in, 16 * 6)
            for k, (n, r, lo, m) in enumerate(units):
                p = loads[n][0]
                if p == 1 and k == first_unit[n]:
                    for t in xw_at(r):
                        xT_out(t)
                    if r <= AHEAD:
                        for c in range(Q - 1):
                            row_sum(r, c)
                    next_sums = list(range(Q - 1)) if AHEAD <= r < T - 1 else []
                high(k)
                if p == 1:
                    while next_sums:
                        row_sum(r + 1, next_sums.pop(0))
                        if k < last_unit[n]:
                            break
                beside(k)
            for k in range(len(units), len(units) + L_NORM):
                beside(k)

        @block.gpsimd
        def _(pool):
            def degree_weights(r):
                pool.wait_ge(rs_act, (Q - 1) * (r + 1))
                pool.wait_ge(rs_dve, r + 1)
                if r >= 1:
                    pool.wait_ge(deg_ok, r)
                pool.tensor_tensor(degw[:, :].rearrange("p (c x) -> p c x", c=Q), same_v,
                                   rs[:, r, :].unsqueeze(2).to_broadcast([P, Q, B]),
                                   ALU.mult).then_inc(degw_ok, 1)

            def root(r):
                pool.wait_ge(degs_ok, r + 1)
                pool.tensor_tensor(D[:, r:r + 1], degs[:, r:r + 1], mhalf[:, :],
                                   ALU.pow).then_inc(D_ok, 1)

            def base(r):
                if r == T - 1:
                    pool.wait_ge(Yl_ok, T)
                    pool.tensor_copy(part[:, r, :], bias[:, :]).then_inc(base_ok, 1)
                    return
                pool.wait_ge(part_ok, r + 1)
                pool.tensor_tensor(part[:, r, :], part[:, r, :], D[:, r:r + 1].to_broadcast([P, H2]),
                                   ALU.mult).then_inc(half_ok, 1)
                pool.wait_ge(half_ok, r + 1)
                pool.tensor_tensor(part[:, r, :], part[:, r, :], bias[:, :], ALU.add).then_inc(base_ok, 1)

            def before_relu(j):
                r = loads[T - 1 + j][1]
                pool.wait_ge(sums_ok, j + 1)
                if j >= 1:
                    pool.wait_ge(relu_ok, j)
                pool.tensor_tensor(hh[:, :], sums[:, 0:H2], sums[:, H2:2 * H2], ALU.add).then_inc(hsum_ok, 1)
                pool.wait_ge(hsum_ok, j + 1)
                pool.tensor_tensor(hh[:, :], hh[:, :], part[:, r, :], ALU.add).then_inc(h_ok, 1)

            def weigh(j):
                r = loads[T - 1 + j][1]
                pool.wait_ge(relu_ok, j + 1)
                if j >= 1:
                    pool.wait_ge(logit_ok, j)
                pool.tensor_tensor(hw[:, :], hr[:, :], watt[:, :], ALU.mult).then_inc(hw_ok, 1)
                if j >= 1:
                    pool.wait_ge(y_ok, j)
                pool.tensor_tensor(dif[:, :], hr[:, 0:H], hr[:, H:H2], ALU.subtract).then_inc(dif_ok, 1)
                pool.tensor_tensor(xs[:, :], xres[:, r, :], hr[:, H:H2], ALU.add).then_inc(xs_ok, 1)

            def join(j):
                pool.wait_ge(gate_ok, j + 1)
                pool.wait_ge(dif_ok, j + 1)
                pool.tensor_tensor(dif[:, :], dif[:, :], lg[:, 1:2].to_broadcast([P, F]),
                                   ALU.mult).then_inc(gated_ok, 1)
                pool.wait_ge(gated_ok, j + 1)
                pool.wait_ge(xs_ok, j + 1)
                if j >= 2:
                    pool.wait_ge(norm_ok, j - 1)
                pool.tensor_tensor(yv[:, j % 2, :], dif[:, :], xs[:, :], ALU.add).then_inc(y_ok, 1)

            def deviation(j):
                pool.wait_ge(aggr_ok, j + 1)
                pool.tensor_tensor(mv[:, j % 2, 2:3], mv[:, j % 2, 1:2], epsc[:, :], ALU.add).then_inc(vare_ok, 1)
                pool.wait_ge(vare_ok, j + 1)
                pool.tensor_tensor(mv[:, j % 2, 3:4], mv[:, j % 2, 2:3], mhalf[:, :],
                                   ALU.pow).then_inc(rstd_ok, 1)

            def loads_before(n):
                raw_free(pool, n)
                load_raw(pool, n, quadrants(n)[1], raw_in_g)

            for n in range(SLOTS):
                loads_before(n)

            same_v = same_x[:, :].rearrange("p (g d) -> p g d", g=Q)
            pool.memset(ident[:, :], 0.0).then_inc(pool_step, 1)
            pool.memset(same_x[:, :], 0.0).then_inc(pool_step, 1)
            pool.memset(ones[:, :], 1.0).then_inc(pool_step, 1)
            pool.memset(mhalf[:, :], -0.5).then_inc(pool_step, 1)
            pool.memset(epsc[:, :], 1e-5).then_inc(pool_step, 1)
            pool.wait_ge(pool_step, 5)
            pool.affine_select(out=ident[:, :], in_=ident[:, :], compare_op=ALU.not_equal, fill=1.0,
                               base=0, pattern=[[-1, P]], channel_multiplier=1).then_inc(pool_const, 1)
            for g in range(Q):
                pool.affine_select(out=same_v, in_=same_v, compare_op=ALU.not_equal, fill=1.0,
                                   base=-B * g, pattern=[[0, Q], [-1, B]],
                                   channel_multiplier=1).then_inc(pool_step, 1)
                pool.wait_ge(pool_step, 6 + g)

            for r in range(T):
                degree_weights(r)
                root(r)
                if r + SLOTS < T:
                    loads_before(r + SLOTS)
                if r >= 2:
                    base(r - 2)
            pool.wait_ge(const_in, 16 * 6)
            base(T - 2)
            base(T - 1)
            for k in range(last_unit[T - 1], len(units) + L_NORM):
                for j in finished(k, L_STATS):
                    deviation(j)
                for j in finished(k, L_GATE):
                    join(j)
                for j in finished(k, L_RELU):
                    weigh(j)
                for j in finished(k, L_SUM):
                    before_relu(j)


_INS = ["x", "adj", "L0_gnn_spatial_x", "L0_gnn_W_f", "L0_gnn_b_f", "L0_gnn_W_s", "L0_gnn_b_s",
        "L0_gnn_W_att", "L0_gnn_b_att"]


def kernel(**inputs):
    import numpy as np
    import concourse.bacc as bacc
    from concourse.bass_utils import run_bass_kernel_spmd

    nc = bacc.Bacc("TRN2", target_bir_lowering=False, num_devices=1)
    arrays, args = {}, []
    for name in _INS:
        a = np.ascontiguousarray(inputs[name])
        arrays[f"in_{name}"] = a
        args.append(nc.dram_tensor(f"in_{name}", a.shape, F32, kind="ExternalInput").ap())
    args.append(nc.dram_tensor("out", arrays["in_x"].shape, F32, kind="ExternalOutput").ap())
    build(nc, *args)
    return run_bass_kernel_spmd(nc, [arrays], core_ids=[0]).results[0]["out"]
```

```python
from contextlib import ExitStack

import concourse.bass as bass
from concourse import mybir

ALU = mybir.AluOpType
ACT = mybir.ActivationFunctionType
AX = mybir.AxisListType
F32 = mybir.dt.float32
F32R = mybir.dt.float32r
BF16 = mybir.dt.bfloat16

P = 128
Q = 4
B = P // Q
UNIT = 8
SLOTS = 3
SPLITS = 3
XB = 4
LEAD = 4
OUT_ROWS = 4


def build(nc, x, adj, sx, W_f, b_f, W_s, b_s, W_att, b_att, out):
    N, F = x.shape
    H = W_f.shape[1]
    H2 = 2 * H
    T = N // P
    CB = N // Q
    assert F == P and H == P and T == CB // B

    late = []
    for a in range(T // 2):
        late += [a] if a == T - 2 - a else [a, T - 2 - a]
    late = late[:T - 1]
    loads = [(1, r) for r in range(T)] + [(2, r) for r in late]

    units, first_unit, last_unit = [], [], []
    for n, (p, r) in enumerate(loads):
        first_unit.append(len(units))
        lo, hi = (0, r + 1) if p == 1 else (r + 1, T)
        for left in range((hi - lo + UNIT - 1) // UNIT, 0, -1):
            m = (hi - lo + left - 1) // left
            units.append((n, r, lo, m))
            lo += m
        last_unit.append(len(units) - 1)
    row_units = [range(first_unit[n], last_unit[n] + 1) for n in range(len(loads))]

    def pair_at(r):
        w = r + LEAD // 2
        return [w] if w < T // 2 else []

    def sums_at(r):
        return ([0] if r == 0 else []) + ([r + 1] if r + 1 < T else [])

    def degrees_before(k):
        rows = []
        for r in range(1, T):
            one = first_unit[r] == last_unit[r]
            if k == (last_unit[r - 1] if one else max(first_unit[r], last_unit[r] - 2)):
                rows.append(r)
        return ([0] if k == 0 else []) + rows

    def halves(m):
        return [(0, UNIT // 2), (UNIT // 2, m)] if m > UNIT // 2 else [(0, m)]

    def half_count(k, h):
        return 2 * k + (1 if h == 0 and len(halves(units[k][3])) == 2 else 2)

    def due(k, lag):
        return [n for n in range(len(loads)) if last_unit[n] + lag == k]

    def finished(k, lag):
        return [n - (T - 1) for n in due(k, lag) if n >= T - 1]

    L_STORE = 1
    L_SUM, L_RELU, L_GATE, L_STATS, L_NORM = 2, 3, 4, 5, 6

    adj_v = adj.rearrange("(c r x) (q y) -> r q x c y", c=Q, x=B, q=Q)
    x_v = x.rearrange("(c r x) f -> c x r f", c=Q, x=B)
    sx_v = sx.rearrange("(c r x) f -> c x r f", c=Q, x=B)
    out_v = out.rearrange("(c r x) f -> c x r f", c=Q, x=B)
    bf_v = b_f.rearrange("(a h) -> a h", a=1).to_broadcast([P, H])
    bs_v = b_s.rearrange("(a h) -> a h", a=1).to_broadcast([P, H])
    watt_v = W_att.rearrange("h a -> a h").to_broadcast([P, H2])
    batt_v = b_att.rearrange("(a h) -> a h", a=1).to_broadcast([P, 1])

    with ExitStack() as ctx:
        def sb(name, shape, dt=F32):
            return ctx.enter_context(nc.sbuf_tensor(name, shape, dt))

        def ps(name, shape, dt=F32):
            return ctx.enter_context(nc.psum_tensor(name, shape, dt))

        def sem(name):
            return ctx.enter_context(nc.semaphore(name))

        Y = sb("Y", [P, T, 2 * H2], F32R)
        part = sb("part", [P, T, H2])
        xres = sb("xres", [P, T, F])
        sxs = sb("sxs", [P, 2, XB, F])
        raw = sb("raw", [P, SLOTS, Q, CB])
        Ah = sb("Ah", [P, SPLITS, UNIT * P], F32R)
        Al = sb("Al", [P, SPLITS, UNIT * P], F32R)
        xT = sb("xT", [P, 4 * P])
        junk = sb("junk", [P, CB], BF16)
        rs = sb("rs", [P, T, Q])
        degw = sb("degw", [P, P])
        degs = sb("degs", [P, T])
        D = sb("D", [P, T])
        ident = sb("ident", [P, P])
        same_x = sb("same_x", [P, P])
        ones = sb("ones", [P, 1])
        mhalf = sb("mhalf", [P, 1])
        epsc = sb("epsc", [P, 1])
        Wfs = sb("Wfs", [P, H2])
        bias = sb("bias", [P, H2])
        watt = sb("watt", [P, H2])
        batt = sb("batt", [P, 1])
        sums = sb("sums", [P, 2 * H2])
        hh = sb("hh", [P, H2])
        hr = sb("hr", [P, H2])
        hw = sb("hw", [P, H2])
        lg = sb("lg", [P, 2])
        dif = sb("dif", [P, F])
        xs = sb("xs", [P, F])
        yv = sb("yv", [P, 2, F])
        st6 = sb("st6", [P, 6])
        mv = sb("mv", [P, 2, 4])

        turned = ps("turned", [P, 2, UNIT * P])
        acc = ps("acc", [P, 2, 2 * H2])
        ps_x = ps("ps_x", [P, 4 * P])
        ps_y = ps("ps_y", [P, 4 * P])

        raw_in = [sem(f"raw_in{i}") for i in range(SLOTS)]
        feat_in = [sem(f"feat_in{i}") for i in range(2)]
        weights_in = sem("weights_in")
        const_in = sem("const_in")
        pool_const = sem("pool_const")
        pool_step = sem("pool_step")
        turned_ok = sem("turned_ok")
        high_ok = sem("high_ok")
        low_ok = sem("low_ok")
        used = sem("used")
        rs_act = sem("rs_act")
        degw_ok = sem("degw_ok")
        deg_ok = sem("deg_ok")
        degs_ok = sem("degs_ok")
        D_ok = sem("D_ok")
        Yh_ok = sem("Yh_ok")
        Yl_ok = sem("Yl_ok")
        xT_ps = sem("xT_ps")
        xT_ok = sem("xT_ok")
        xw_ps = sem("xw_ps")
        xw_ok = sem("xw_ok")
        part_ok = sem("part_ok")
        base_ok = sem("base_ok")
        half_ok = sem("half_ok")
        sums_ok = sem("sums_ok")
        hsum_ok = sem("hsum_ok")
        h_ok = sem("h_ok")
        relu_ok = sem("relu_ok")
        hw_ok = sem("hw_ok")
        logit_ok = sem("logit_ok")
        gate_ok = sem("gate_ok")
        dif_ok = sem("dif_ok")
        xs_ok = sem("xs_ok")
        gated_ok = sem("gated_ok")
        y_ok = sem("y_ok")
        stats_ok = sem("stats_ok")
        aggr_ok = sem("aggr_ok")
        vare_ok = sem("vare_ok")
        rstd_ok = sem("rstd_ok")
        norm_ok = sem("norm_ok")
        stored = sem("stored")

        block = ctx.enter_context(nc.Block())

        def raw_free(eng, n):
            if n < SLOTS:
                return
            p, r = loads[n - SLOTS]
            eng.wait_ge(turned_ok, 2 * (last_unit[n - SLOTS] + 1))
            if p == 1:
                eng.wait_ge(rs_act, Q * (r + 1))

        SYNC_QUADRANTS, ACT_QUADRANTS = (0, 1), (2, 3)

        def load_raw(eng, n, quadrants):
            p, r = loads[n]
            y0 = 0 if p == 1 else B * (r + 1)
            for q in quadrants:
                eng.dma_start(raw[B * q:B * (q + 1), n % SLOTS, :, y0:CB],
                              adj_v[r, q, :, :, y0:CB]).then_inc(raw_in[n % SLOTS], 16)

        def raw_here(eng, n):
            eng.wait_ge(raw_in[n % SLOTS], 16 * Q * (n // SLOTS + 1))

        def load_features(eng, m):
            if m >= 2:
                eng.wait_ge(xT_ps, XB // 2 * (m - 1))
            for c in range(Q):
                eng.dma_start(xres[B * c:B * (c + 1), XB * m:XB * (m + 1), :],
                              x_v[c, :, XB * m:XB * (m + 1), :]).then_inc(feat_in[m % 2], 16)
                eng.dma_start(sxs[B * c:B * (c + 1), m % 2, :, :],
                              sx_v[c, :, XB * m:XB * (m + 1), :]).then_inc(feat_in[m % 2], 16)

        stores, done = [], set()
        for j in range(T):
            r = loads[T - 1 + j][1]
            done.add(r)
            a = OUT_ROWS * (r // OUT_ROWS)
            if done >= set(range(a, a + OUT_ROWS)):
                stores.append((j + 1, a))

        @block.sync
        def _(sp):
            load_features(sp, 0)
            sp.dma_start(Wfs[:, 0:H], W_f).then_inc(weights_in, 16)
            sp.dma_start(Wfs[:, H:H2], W_s).then_inc(weights_in, 16)
            load_raw(sp, 0, SYNC_QUADRANTS)
            sp.dma_start(bias[:, 0:H], bf_v).then_inc(const_in, 16)
            sp.dma_start(bias[:, H:H2], bs_v).then_inc(const_in, 16)
            sp.dma_start(watt[:, :], watt_v).then_inc(const_in, 16)
            sp.dma_start(batt[:, :], batt_v).then_inc(const_in, 16)
            load_features(sp, 1)
            for n in range(1, len(loads)):
                raw_free(sp, n)
                load_raw(sp, n, SYNC_QUADRANTS)
                if n % 2 == 0 and n // 2 + 1 < T // XB:
                    load_features(sp, n // 2 + 1)
            for j, a in stores:
                sp.wait_ge(norm_ok, j)
                for c in range(Q):
                    sp.dma_start(out_v[c, :, a:a + OUT_ROWS, :],
                                 part[B * c:B * (c + 1), a:a + OUT_ROWS, 0:F]).then_inc(stored, 16)
            sp.wait_ge(stored, 16 * Q * len(stores))

        @block.tensor
        def _(pe):
            def turn_features(w, degrees):
                m = 2 * w // XB
                pe.wait_ge(feat_in[m % 2], 32 * Q * (m // 2 + 1))
                if w >= 1:
                    pe.wait_ge(xT_ok, w)
                if degrees:
                    pe.wait_ge(degs_ok, degrees)
                for i in range(2):
                    t = 2 * w + i
                    pe.transpose(ps_x[:, 2 * i * P:(2 * i + 1) * P], xres[:, t, :], ident[:, :])
                    tr = pe.transpose(ps_x[:, (2 * i + 1) * P:(2 * i + 2) * P], sxs[:, m % 2, t % XB, :],
                                      ident[:, :])
                tr.then_inc(xT_ps, 1)

            def xw(w):
                pe.wait_ge(xT_ok, w + 1)
                if w >= 1:
                    pe.wait_ge(xw_ok, w)
                for i in range(4):
                    mm = pe.matmul(ps_y[:, i * P:(i + 1) * P], xT[:, i * P:(i + 1) * P],
                                   Wfs[:, (i % 2) * H:(i % 2 + 1) * H], start=True, stop=True)
                mm.then_inc(xw_ps, 1)

            def degree(r, pairs):
                pe.wait_ge(degw_ok, r + 1)
                pe.wait_ge(xT_ok, pairs)
                if r >= 1:
                    pe.wait_ge(degs_ok, r)
                pe.matmul(ps_x[:, 0:1], degw[:, :], ones[:, :], start=True, stop=True).then_inc(deg_ok, 1)

            def multiply(k, first, last):
                n, _, lo, m = units[k]
                for i in range(m):
                    t = lo + i
                    if i % (UNIT // 2) == 0:
                        pe.wait_ge(low_ok, half_count(k, i // (UNIT // 2)))
                    pe.matmul(acc[:, n % 2, :], Ah[:, k % SPLITS, i * P:(i + 1) * P], Y[:, t, :],
                              start=(first and i == 0), stop=False)
                    mm = pe.matmul(acc[:, n % 2, 0:H2], Al[:, k % SPLITS, i * P:(i + 1) * P],
                                   Y[:, t, 0:H2], start=False, stop=(last and i == m - 1))
                mm.then_inc(used, 1)

            pe.wait_ge(pool_const, 1)
            pe.wait_ge(weights_in, 16 * 2)
            for w in range(LEAD // 2):
                turn_features(w, 0)
                xw(w)
            pairs, degrees = LEAD // 2, 0
            for n, (p, r) in enumerate(loads):
                if p == 1 and r >= 1:
                    for w in pair_at(r - 1):
                        xw(w)
                if 2 <= n < T + 1:
                    pe.wait_ge(part_ok, n - 1)
                elif n >= T + 1:
                    pe.wait_ge(sums_ok, n - T)
                for k in row_units[n]:
                    if p == 1 and k == last_unit[n]:
                        for w in pair_at(r):
                            turn_features(w, degrees)
                            pairs = w + 1
                    for d in degrees_before(k):
                        degree(d, pairs)
                        degrees = d + 1
                    if p == 1 and k == last_unit[n]:
                        pe.wait_ge(Yl_ok, r + 1)
                    multiply(k, k == first_unit[n], k == last_unit[n])

        @block.vector
        def _(dve):
            def turn(k, h):
                n, r, lo, m = units[k]
                i, j = halves(m)[h]
                if k == first_unit[n] and h == 0:
                    raw_here(dve, n)
                if k >= 2:
                    dve.wait_ge(high_ok, k - 1)
                    dve.wait_ge(low_ok, half_count(k - 2, h))
                src = raw[:, n % SLOTS, :, (lo + i) * B:(lo + j) * B].rearrange("p c (t y) -> p t c y", y=B)
                dst = turned[:, k % 2, i * P:j * P].rearrange("p (t c x) -> p t c x", c=Q, x=B)
                dve.transpose(dst, src).then_inc(turned_ok, 3 - len(halves(m)))

            def low(k, h):
                m = units[k][3]
                i, j = halves(m)[h]
                if h == 0:
                    dve.wait_ge(high_ok, k + 1)
                    if k >= SPLITS:
                        dve.wait_ge(used, k - SPLITS + 1)
                dve.tensor_tensor(Al[:, k % SPLITS, i * P:j * P], turned[:, k % 2, i * P:j * P],
                                  Ah[:, k % SPLITS, i * P:j * P],
                                  ALU.subtract).then_inc(low_ok, 3 - len(halves(m)))

            def xw_out(w):
                dve.wait_ge(xw_ps, w + 1)
                dve.tensor_copy(part[:, 2 * w:2 * w + 2, :],
                                ps_y[:, :].rearrange("p (t h) -> p t h", t=2)).then_inc(xw_ok, 1)

            def take_degrees(r):
                dve.wait_ge(deg_ok, r + 1)
                dve.tensor_scalar(degs[:, r:r + 1], ps_x[:, 0:1], 1e-9, None,
                                  ALU.add).then_inc(degs_ok, 1)

            def scale_y(r):
                dve.wait_ge(D_ok, r + 1)
                dve.wait_ge(xw_ok, r // 2 + 1)
                dve.tensor_scalar(Y[:, r, 0:H2], part[:, r, :], D[:, r:r + 1], None,
                                  ALU.mult).then_inc(Yh_ok, 1)
                dve.wait_ge(Yh_ok, r + 1)
                dve.scalar_tensor_tensor(out=Y[:, r, H2:2 * H2], in0=part[:, r, :], scalar=D[:, r:r + 1],
                                         in1=Y[:, r, 0:H2], op0=ALU.mult,
                                         op1=ALU.subtract).then_inc(Yl_ok, 1)

            def store_part(n):
                dve.wait_ge(used, last_unit[n] + 1)
                dve.wait_ge(Yl_ok, n + 1)
                dve.tensor_reduce(part[:, n, :], acc[:, n % 2, :].rearrange("p (a h) -> p h a", a=2), AX.X,
                                  ALU.add).then_inc(part_ok, 1)

            def stats(j):
                dve.wait_ge(y_ok, j + 1)
                if j >= 1:
                    dve.wait_ge(aggr_ok, j)
                dve.bn_stats(st6[:, :], yv[:, j % 2, :]).then_inc(stats_ok, 1)
                dve.wait_ge(stats_ok, j + 1)
                if j >= 2:
                    dve.wait_ge(norm_ok, j - 1)
                dve.bn_aggr(mv[:, j % 2, 0:2], st6[:, :]).then_inc(aggr_ok, 1)

            def normalise(j):
                r = loads[T - 1 + j][1]
                dve.wait_ge(rstd_ok, j + 1)
                dve.tensor_scalar(part[:, r, 0:F], yv[:, j % 2, :], mv[:, j % 2, 0:1], mv[:, j % 2, 3:4],
                                  ALU.subtract, ALU.mult).then_inc(norm_ok, 1)

            def beside(k):
                for n in due(k, L_STORE):
                    if n < T - 1:
                        store_part(n)
                for j in finished(k, L_NORM):
                    normalise(j)
                for j in finished(k, L_STATS):
                    stats(j)

            for w in range(LEAD // 2):
                xw_out(w)
            for k, (n, r, lo, m) in enumerate(units):
                p = loads[n][0]
                for h in range(2):
                    if h < len(halves(m)):
                        turn(k, h)
                    if k >= 1 and h < len(halves(units[k - 1][3])):
                        low(k - 1, h)
                if k >= 1:
                    beside(k - 1)
                if p == 1 and k == max(first_unit[n], last_unit[n] - 1):
                    take_degrees(r)
                if p == 1 and k == last_unit[n]:
                    if r >= 1:
                        for w in pair_at(r - 1):
                            xw_out(w)
                    scale_y(r)
            for h in range(len(halves(units[-1][3]))):
                low(len(units) - 1, h)
            for k in range(len(units) - 1, len(units) + L_NORM):
                beside(k)

        @block.scalar
        def _(act):
            junk_writes = [0, 0]

            def junk_free():
                if junk_writes[0]:
                    act.wait_ge(rs_act, junk_writes[0])
                if junk_writes[1]:
                    act.wait_ge(logit_ok, junk_writes[1])

            def high(k):
                m = units[k][3]
                act.wait_ge(turned_ok, 2 * (k + 1))
                if k >= SPLITS:
                    act.wait_ge(used, k - SPLITS + 1)
                act.activation(Ah[:, k % SPLITS, 0:m * P], turned[:, k % 2, 0:m * P],
                               ACT.Copy).then_inc(high_ok, 1)

            def row_sum(r, c):
                raw_here(act, r)
                junk_free()
                junk_writes[0] += 1
                act.activation(junk[:, 0:CB], raw[:, r % SLOTS, c, :], ACT.Copy,
                               accum_out=rs[:, r, c:c + 1]).then_inc(rs_act, 1)

            def xT_out(w):
                act.wait_ge(xT_ps, w + 1)
                if w >= 1:
                    act.wait_ge(xw_ps, w)
                act.activation(xT[:, :], ps_x[:, :], ACT.Copy).then_inc(xT_ok, 1)

            def evacuate(j):
                n = T - 1 + j
                r = loads[n][1]
                act.wait_ge(used, last_unit[n] + 1)
                act.wait_ge(D_ok, r + 1)
                if j >= 1:
                    act.wait_ge(hsum_ok, j)
                act.activation(sums[:, :], acc[:, n % 2, :], ACT.Copy,
                               scale=D[:, r:r + 1]).then_inc(sums_ok, 1)

            def relu(j):
                act.wait_ge(h_ok, j + 1)
                if j >= 1:
                    act.wait_ge(xs_ok, j)
                act.activation(hr[:, :], hh[:, :], ACT.Relu).then_inc(relu_ok, 1)

            def gate(j):
                act.wait_ge(hw_ok, j + 1)
                if j >= 1:
                    act.wait_ge(gate_ok, j)
                junk_free()
                junk_writes[1] += 1
                act.activation(junk[:, 0:H2], hw[:, :], ACT.Copy,
                               accum_out=lg[:, 0:1]).then_inc(logit_ok, 1)
                act.wait_ge(logit_ok, j + 1)
                if j >= 1:
                    act.wait_ge(gated_ok, j)
                act.activation(lg[:, 1:2], lg[:, 0:1], ACT.Sigmoid, bias=batt[:, :]).then_inc(gate_ok, 1)

            def beside(k):
                for j in finished(k, L_GATE):
                    gate(j)
                for j in finished(k, L_RELU):
                    relu(j)
                for j in finished(k, L_SUM):
                    evacuate(j)

            for n in range(SLOTS):
                load_raw(act, n, ACT_QUADRANTS)
            for w in range(LEAD // 2):
                xT_out(w)
            act.wait_ge(const_in, 16 * 4)
            for k, (n, r, lo, m) in enumerate(units):
                p = loads[n][0]
                if p == 1 and k == first_unit[n]:
                    todo = [(d, c) for d in sums_at(r) for c in range(Q)]
                    if r == 0:
                        for c in range(Q):
                            row_sum(*todo.pop(0))
                high(k)
                if p == 1:
                    while todo:
                        row_sum(*todo.pop(0))
                        if k < last_unit[n]:
                            break
                    if k == last_unit[n]:
                        for w in pair_at(r):
                            xT_out(w)
                if k == last_unit[n] and n + SLOTS < len(loads):
                    raw_free(act, n + SLOTS)
                    load_raw(act, n + SLOTS, ACT_QUADRANTS)
                beside(k)
            for k in range(len(units), len(units) + L_NORM):
                beside(k)

        @block.gpsimd
        def _(pool):
            def degree_weights(r):
                pool.wait_ge(rs_act, Q * (r + 1))
                if r >= 1:
                    pool.wait_ge(deg_ok, r)
                pool.tensor_tensor(degw[:, :].rearrange("p (c x) -> p c x", c=Q), same_v,
                                   rs[:, r, :].unsqueeze(2).to_broadcast([P, Q, B]),
                                   ALU.mult).then_inc(degw_ok, 1)

            def root(r):
                pool.wait_ge(degs_ok, r + 1)
                pool.tensor_tensor(D[:, r:r + 1], degs[:, r:r + 1], mhalf[:, :],
                                   ALU.pow).then_inc(D_ok, 1)

            def base(r):
                if r == T - 1:
                    pool.wait_ge(Yl_ok, T)
                    pool.tensor_copy(part[:, r, :], bias[:, :]).then_inc(base_ok, 1)
                    return
                pool.wait_ge(part_ok, r + 1)
                pool.tensor_tensor(part[:, r, :], part[:, r, :], D[:, r:r + 1].to_broadcast([P, H2]),
                                   ALU.mult).then_inc(half_ok, 1)
                pool.wait_ge(half_ok, r + 1)
                pool.tensor_tensor(part[:, r, :], part[:, r, :], bias[:, :], ALU.add).then_inc(base_ok, 1)

            def before_relu(j):
                r = loads[T - 1 + j][1]
                pool.wait_ge(sums_ok, j + 1)
                if j >= 1:
                    pool.wait_ge(relu_ok, j)
                pool.tensor_tensor(hh[:, :], sums[:, 0:H2], sums[:, H2:2 * H2], ALU.add).then_inc(hsum_ok, 1)
                pool.wait_ge(hsum_ok, j + 1)
                pool.tensor_tensor(hh[:, :], hh[:, :], part[:, r, :], ALU.add).then_inc(h_ok, 1)

            def weigh(j):
                r = loads[T - 1 + j][1]
                pool.wait_ge(relu_ok, j + 1)
                if j >= 1:
                    pool.wait_ge(logit_ok, j)
                pool.tensor_tensor(hw[:, :], hr[:, :], watt[:, :], ALU.mult).then_inc(hw_ok, 1)
                if j >= 1:
                    pool.wait_ge(y_ok, j)
                pool.tensor_tensor(dif[:, :], hr[:, 0:H], hr[:, H:H2], ALU.subtract).then_inc(dif_ok, 1)
                pool.tensor_tensor(xs[:, :], xres[:, r, :], hr[:, H:H2], ALU.add).then_inc(xs_ok, 1)

            def join(j):
                pool.wait_ge(gate_ok, j + 1)
                pool.wait_ge(dif_ok, j + 1)
                pool.tensor_tensor(dif[:, :], dif[:, :], lg[:, 1:2].to_broadcast([P, F]),
                                   ALU.mult).then_inc(gated_ok, 1)
                pool.wait_ge(gated_ok, j + 1)
                pool.wait_ge(xs_ok, j + 1)
                if j >= 2:
                    pool.wait_ge(norm_ok, j - 1)
                pool.tensor_tensor(yv[:, j % 2, :], dif[:, :], xs[:, :], ALU.add).then_inc(y_ok, 1)

            def deviation(j):
                pool.wait_ge(aggr_ok, j + 1)
                pool.tensor_tensor(mv[:, j % 2, 2:3], mv[:, j % 2, 1:2], epsc[:, :], ALU.add).then_inc(vare_ok, 1)
                pool.wait_ge(vare_ok, j + 1)
                pool.tensor_tensor(mv[:, j % 2, 3:4], mv[:, j % 2, 2:3], mhalf[:, :],
                                   ALU.pow).then_inc(rstd_ok, 1)

            same_v = same_x[:, :].rearrange("p (g d) -> p g d", g=Q)
            pool.memset(ident[:, :], 0.0).then_inc(pool_step, 1)
            pool.memset(same_x[:, :], 0.0).then_inc(pool_step, 1)
            pool.memset(ones[:, :], 1.0).then_inc(pool_step, 1)
            pool.memset(mhalf[:, :], -0.5).then_inc(pool_step, 1)
            pool.memset(epsc[:, :], 1e-5).then_inc(pool_step, 1)
            pool.wait_ge(pool_step, 5)
            pool.affine_select(out=ident[:, :], in_=ident[:, :], compare_op=ALU.not_equal, fill=1.0,
                               base=0, pattern=[[-1, P]], channel_multiplier=1).then_inc(pool_const, 1)
            for g in range(Q):
                pool.affine_select(out=same_v, in_=same_v, compare_op=ALU.not_equal, fill=1.0,
                                   base=-B * g, pattern=[[0, Q], [-1, B]],
                                   channel_multiplier=1).then_inc(pool_step, 1)
                pool.wait_ge(pool_step, 6 + g)

            for r in range(T):
                degree_weights(r)
                root(r)
                if r >= 2:
                    base(r - 2)
            pool.wait_ge(const_in, 16 * 4)
            base(T - 2)
            base(T - 1)
            for k in range(last_unit[T - 1], len(units) + L_NORM):
                for j in finished(k, L_STATS):
                    deviation(j)
                for j in finished(k, L_GATE):
                    join(j)
                for j in finished(k, L_RELU):
                    weigh(j)
                for j in finished(k, L_SUM):
                    before_relu(j)


_INS = ["x", "adj", "L0_gnn_spatial_x", "L0_gnn_W_f", "L0_gnn_b_f", "L0_gnn_W_s", "L0_gnn_b_s",
        "L0_gnn_W_att", "L0_gnn_b_att"]


def kernel(**inputs):
    import numpy as np
    import concourse.bacc as bacc
    from concourse.bass_utils import run_bass_kernel_spmd

    nc = bacc.Bacc("TRN2", target_bir_lowering=False, num_devices=1)
    arrays, args = {}, []
    for name in _INS:
        a = np.ascontiguousarray(inputs[name])
        arrays[f"in_{name}"] = a
        args.append(nc.dram_tensor(f"in_{name}", a.shape, F32, kind="ExternalInput").ap())
    args.append(nc.dram_tensor("out", arrays["in_x"].shape, F32, kind="ExternalOutput").ap())
    build(nc, *args)
    return run_bass_kernel_spmd(nc, [arrays], core_ids=[0]).results[0]["out"]
```

```python
from contextlib import ExitStack

import concourse.bass as bass
from concourse import mybir

ALU = mybir.AluOpType
ACT = mybir.ActivationFunctionType
AX = mybir.AxisListType
F32 = mybir.dt.float32
F32R = mybir.dt.float32r
BF16 = mybir.dt.bfloat16

P = 128
Q = 4
B = P // Q
UNIT = 8
SLOTS = 3
SPLITS = 3
XB = 4
LEAD = 4
ROWS = 4
OUT_ROWS = 4


def build(nc, x, adj, sx, W_f, b_f, W_s, b_s, W_att, b_att, out):
    N, F = x.shape
    H = W_f.shape[1]
    H2 = 2 * H
    T = N // P
    CB = N // Q
    assert F == P and H == P and T == CB // B

    late = []
    for a in range(T // 2):
        late += [a] if a == T - 2 - a else [a, T - 2 - a]
    late = late[:T - 1]
    loads = [(1, r) for r in range(T)] + [(2, r) for r in late]

    units, first_unit, last_unit = [], [], []
    for n, (p, r) in enumerate(loads):
        first_unit.append(len(units))
        lo, hi = (0, r + 1) if p == 1 else (r + 1, T)
        for left in range((hi - lo + UNIT - 1) // UNIT, 0, -1):
            m = (hi - lo + left - 1) // left
            units.append((n, r, lo, m))
            lo += m
        last_unit.append(len(units) - 1)
    row_units = [range(first_unit[n], last_unit[n] + 1) for n in range(len(loads))]

    def pair_at(r):
        w = r + LEAD // 2
        return [w] if w < T // 2 else []

    def sums_after(k):
        n, r = units[k][:2]
        if loads[n][0] == 2:
            return []
        spread = {1: [4], 2: [2, 2], 3: [1, 1, 1], 4: [1, 1, 1, 1]}[len(row_units[n])]
        i = k - first_unit[n]
        sums = [(r, Q - 1)] if i == 0 and r > 0 and len(row_units[n - 1]) == 3 else []
        if r + 1 < T:
            sums += [(r + 1, c) for c in range(sum(spread[:i]), sum(spread[:i + 1]))]
        return [(d, c) for d, c in sums if d > 1]

    def degrees_before(k):
        rows = []
        for r in range(1, T):
            one = first_unit[r] == last_unit[r]
            if k == (last_unit[r - 1] if one else last_unit[r] - (1 if len(row_units[r]) < 4 else 2)):
                rows.append(r)
        return ([0] if k == 0 else []) + rows

    K2 = first_unit[T]

    def buffer(k):
        return k % 2 if k < K2 else (2, K2 % 2, 1 - K2 % 2)[(k - K2) % 3]

    def before_in_buffer(k):
        return max((j for j in range(max(0, k - 3), k) if buffer(j) == buffer(k)), default=None)

    def pieces(k):
        m = units[k][3]
        return [(0, UNIT // 2), (UNIT // 2, m)] if m > UNIT // 2 and k < K2 else [(0, m)]

    def piece_count(k, h):
        return 2 * k + (1 if h == 0 and len(pieces(k)) == 2 else 2)

    def due(k, lag):
        return [n for n in range(len(loads)) if last_unit[n] + lag == k]

    def finished(k, lag):
        return [n - (T - 1) for n in due(k, lag) if n >= T - 1]

    L_STORE = 1
    L_SUM, L_RELU, L_GATE, L_STATS, L_NORM = 2, 4, 6, 8, 9

    H_F, H_S, H_ALL = slice(0, H), slice(H, H2), slice(0, H2)
    Y_OUT, XS = slice(H2, H2 + F), slice(H2 + F, H2 + 2 * F)

    adj_v = adj.rearrange("(c r x) (q y) -> r q x c y", c=Q, x=B, q=Q)
    x_v = x.rearrange("(c r x) f -> c x r f", c=Q, x=B)
    sx_v = sx.rearrange("(c r x) f -> c x r f", c=Q, x=B)
    out_v = out.rearrange("(c r x) f -> c x r f", c=Q, x=B)
    bf_v = b_f.rearrange("(a h) -> a h", a=1).to_broadcast([P, H])
    bs_v = b_s.rearrange("(a h) -> a h", a=1).to_broadcast([P, H])
    watt_v = W_att.rearrange("h a -> a h").to_broadcast([P, H2])
    batt_v = b_att.rearrange("(a h) -> a h", a=1).to_broadcast([P, 1])

    with ExitStack() as ctx:
        def sb(name, shape, dt=F32):
            return ctx.enter_context(nc.sbuf_tensor(name, shape, dt))

        def ps(name, shape, dt=F32):
            return ctx.enter_context(nc.psum_tensor(name, shape, dt))

        def sem(name):
            return ctx.enter_context(nc.semaphore(name))

        Y = sb("Y", [P, T, 2 * H2], F32R)
        part = sb("part", [P, T, H2])
        xres = sb("xres", [P, T, F])
        sxs = sb("sxs", [P, 2, XB, F])
        raw = sb("raw", [P, SLOTS, Q, CB])
        Ah = sb("Ah", [P, SPLITS, UNIT * P], F32R)
        Al = sb("Al", [P, SPLITS, UNIT * P], F32R)
        xT = sb("xT", [P, 4 * P])
        junk = sb("junk", [P, 2, CB], BF16)
        rs = sb("rs", [P, T, Q])
        degw = sb("degw", [P, P])
        degs = sb("degs", [P, T])
        D = sb("D", [P, T])
        ident = sb("ident", [P, P])
        same_x = sb("same_x", [P, P])
        ones = sb("ones", [P, 1])
        mhalf = sb("mhalf", [P, 1])
        epsc = sb("epsc", [P, 1])
        Wfs = sb("Wfs", [P, H2])
        bias = sb("bias", [P, H2])
        watt = sb("watt", [P, H2])
        batt = sb("batt", [P, 1])
        fin = sb("fin", [P, ROWS, 2 * H2])
        lg = sb("lg", [P, ROWS, 2])
        st6 = sb("st6", [P, 6])
        mv = sb("mv", [P, ROWS, 4])

        turned = ps("turned", [P, 3, UNIT * P])
        acc = ps("acc", [P, 2, 2 * H2])
        ps_x = turned[:, 2, 0:4 * P]
        ps_y = turned[:, 2, 4 * P:8 * P]

        raw_in = [sem(f"raw_in{i}") for i in range(SLOTS)]
        feat_in = [sem(f"feat_in{i}") for i in range(2)]
        weights_in = sem("weights_in")
        const_in = sem("const_in")
        pool_const = sem("pool_const")
        pool_step = sem("pool_step")
        turned_ok = sem("turned_ok")
        high_ok = sem("high_ok")
        low_ok = sem("low_ok")
        used = sem("used")
        rs_act = sem("rs_act")
        degw_ok = sem("degw_ok")
        deg_ok = sem("deg_ok")
        degs_ok = sem("degs_ok")
        D_ok = sem("D_ok")
        Yh_ok = sem("Yh_ok")
        Yl_ok = sem("Yl_ok")
        xT_ps = sem("xT_ps")
        xT_ok = sem("xT_ok")
        xw_ps = sem("xw_ps")
        xw_ok = sem("xw_ok")
        part_ok = sem("part_ok")
        base_ok = sem("base_ok")
        whole_ok = sem("whole_ok")
        sums_ok = sem("sums_ok")
        h_ok = sem("h_ok")
        relu_ok = sem("relu_ok")
        hw_ok = sem("hw_ok")
        logit_ok = sem("logit_ok")
        gate_ok = sem("gate_ok")
        dif_ok = sem("dif_ok")
        xs_ok = sem("xs_ok")
        gated_ok = sem("gated_ok")
        y_ok = sem("y_ok")
        stats_ok = sem("stats_ok")
        aggr_ok = sem("aggr_ok")
        vare_ok = sem("vare_ok")
        rstd_ok = sem("rstd_ok")
        norm_ok = sem("norm_ok")
        stored = sem("stored")

        block = ctx.enter_context(nc.Block())

        def raw_free(eng, n):
            if n < SLOTS:
                return
            p, r = loads[n - SLOTS]
            eng.wait_ge(turned_ok, 2 * (last_unit[n - SLOTS] + 1))
            if p == 1:
                eng.wait_ge(rs_act, Q * (r + 1))

        SYNC_QUADRANTS, ACT_QUADRANTS = (0, 1), (2, 3)

        def load_raw(eng, n, quadrants):
            p, r = loads[n]
            y0 = 0 if p == 1 else B * (r + 1)
            for q in quadrants:
                eng.dma_start(raw[B * q:B * (q + 1), n % SLOTS, :, y0:CB],
                              adj_v[r, q, :, :, y0:CB]).then_inc(raw_in[n % SLOTS], 16)

        def raw_here(eng, n):
            eng.wait_ge(raw_in[n % SLOTS], 16 * Q * (n // SLOTS + 1))

        def load_features(eng, m):
            if m >= 2:
                eng.wait_ge(xT_ps, XB // 2 * (m - 1))
            for c in range(Q):
                eng.dma_start(xres[B * c:B * (c + 1), XB * m:XB * (m + 1), :],
                              x_v[c, :, XB * m:XB * (m + 1), :]).then_inc(feat_in[m % 2], 16)
                eng.dma_start(sxs[B * c:B * (c + 1), m % 2, :, :],
                              sx_v[c, :, XB * m:XB * (m + 1), :]).then_inc(feat_in[m % 2], 16)

        groups = [range(max(0, a), min(T, a + OUT_ROWS)) for a in range(1 - OUT_ROWS, T, OUT_ROWS)]
        stores, done = [], set()
        for j in range(T):
            done.add(loads[T - 1 + j][1])
            for group in groups:
                if done >= set(group) and loads[T - 1 + j][1] in group:
                    stores.append((j + 1, group[0], group[-1] + 1))

        @block.sync
        def _(sp):
            load_raw(sp, 0, SYNC_QUADRANTS)
            load_features(sp, 0)
            sp.dma_start(Wfs[:, 0:H], W_f).then_inc(weights_in, 16)
            sp.dma_start(Wfs[:, H:H2], W_s).then_inc(weights_in, 16)
            sp.dma_start(bias[:, 0:H], bf_v).then_inc(const_in, 16)
            sp.dma_start(bias[:, H:H2], bs_v).then_inc(const_in, 16)
            sp.dma_start(watt[:, :], watt_v).then_inc(const_in, 16)
            sp.dma_start(batt[:, :], batt_v).then_inc(const_in, 16)
            load_features(sp, 1)
            for n in range(1, len(loads)):
                raw_free(sp, n)
                load_raw(sp, n, SYNC_QUADRANTS)
                if n % 2 == 0 and n // 2 + 1 < T // XB:
                    load_features(sp, n // 2 + 1)
            for j, a, b in stores:
                sp.wait_ge(norm_ok, j)
                for c in range(Q):
                    sp.dma_start(out_v[c, :, a:b, :],
                                 part[B * c:B * (c + 1), a:b, 0:F]).then_inc(stored, 16)
            sp.wait_ge(stored, 16 * Q * len(stores))

        def add_base(eng, j):
            r = loads[T - 1 + j][1]
            eng.wait_ge(sums_ok, j + 1)
            if j == 0:
                eng.wait_ge(base_ok, 1)
            else:
                eng.wait_ge(part_ok, r + 1)
            eng.tensor_tensor(fin[:, j % ROWS, H_ALL], fin[:, j % ROWS, H_ALL], part[:, r, :],
                              ALU.add).then_inc(h_ok, 1)

        def weigh(eng, j):
            r = loads[T - 1 + j][1]
            f = fin[:, j % ROWS, :]
            eng.wait_ge(relu_ok, j + 1)
            eng.tensor_tensor(f[:, Y_OUT], f[:, H_F], f[:, H_S], ALU.subtract).then_inc(dif_ok, 1)
            eng.tensor_tensor(f[:, XS], xres[:, r, :], f[:, H_S], ALU.add).then_inc(xs_ok, 1)
            eng.wait_ge(dif_ok, j + 1)
            eng.wait_ge(xs_ok, j + 1)
            eng.tensor_tensor(f[:, H_ALL], f[:, H_ALL], watt[:, :], ALU.mult).then_inc(hw_ok, 1)

        def join(eng, j):
            f = fin[:, j % ROWS, :]
            eng.wait_ge(gate_ok, j + 1)
            eng.wait_ge(dif_ok, j + 1)
            eng.tensor_tensor(f[:, Y_OUT], f[:, Y_OUT], lg[:, j % ROWS, 1:2].to_broadcast([P, F]),
                              ALU.mult).then_inc(gated_ok, 1)
            eng.wait_ge(gated_ok, j + 1)
            eng.wait_ge(xs_ok, j + 1)
            eng.tensor_tensor(f[:, Y_OUT], f[:, Y_OUT], f[:, XS], ALU.add).then_inc(y_ok, 1)

        @block.tensor
        def _(pe):
            def turn_features(w, degrees):
                m = 2 * w // XB
                pe.wait_ge(feat_in[m % 2], 32 * Q * (m // 2 + 1))
                if w >= 1:
                    pe.wait_ge(xT_ok, w)
                if degrees:
                    pe.wait_ge(degs_ok, degrees)
                for i in range(2):
                    t = 2 * w + i
                    pe.transpose(ps_x[:, 2 * i * P:(2 * i + 1) * P], xres[:, t, :], ident[:, :])
                    tr = pe.transpose(ps_x[:, (2 * i + 1) * P:(2 * i + 2) * P], sxs[:, m % 2, t % XB, :],
                                      ident[:, :])
                tr.then_inc(xT_ps, 1)

            def xw(w):
                pe.wait_ge(xT_ok, w + 1)
                if w >= 1:
                    pe.wait_ge(xw_ok, w)
                for i in range(4):
                    mm = pe.matmul(ps_y[:, i * P:(i + 1) * P], xT[:, i * P:(i + 1) * P],
                                   Wfs[:, (i % 2) * H:(i % 2 + 1) * H], start=True, stop=True)
                mm.then_inc(xw_ps, 1)

            def degree(r, pairs):
                pe.wait_ge(degw_ok, r + 1)
                pe.wait_ge(xT_ok, pairs)
                if r >= 1:
                    pe.wait_ge(degs_ok, r)
                pe.matmul(ps_x[:, 0:1], degw[:, :], ones[:, :], start=True, stop=True).then_inc(deg_ok, 1)

            def multiply(k, first, last):
                n, r, lo, m = units[k]
                for i in range(m):
                    t = lo + i
                    for h, (a, b) in enumerate(pieces(k)):
                        if i == a:
                            pe.wait_ge(low_ok, piece_count(k, h))
                    if t == r:
                        pe.wait_ge(Yl_ok, r + 1)
                    pe.matmul(acc[:, n % 2, 0:H2], Ah[:, k % SPLITS, i * P:(i + 1) * P], Y[:, t, 0:H2],
                              start=(first and i == 0), stop=False)
                    pe.matmul(acc[:, n % 2, 0:H2], Ah[:, k % SPLITS, i * P:(i + 1) * P], Y[:, t, H2:2 * H2],
                              start=False, stop=False)
                    mm = pe.matmul(acc[:, n % 2, 0:H2], Al[:, k % SPLITS, i * P:(i + 1) * P],
                                   Y[:, t, 0:H2], start=False, stop=(last and i == m - 1))
                mm.then_inc(used, 1)

            pe.wait_ge(pool_const, 1)
            pe.wait_ge(weights_in, 16 * 2)
            for w in range(LEAD // 2):
                turn_features(w, 0)
                xw(w)
            pairs, degrees = LEAD // 2, 0
            for n, (p, r) in enumerate(loads):
                if p == 1 and r >= 1:
                    for w in pair_at(r - 1):
                        xw(w)
                if 2 <= n < T + 1:
                    pe.wait_ge(part_ok, n - 1)
                elif n >= T + 1:
                    pe.wait_ge(sums_ok, n - T)
                for k in row_units[n]:
                    if p == 1 and k == last_unit[n]:
                        for w in pair_at(r):
                            turn_features(w, degrees)
                            pairs = w + 1
                    for d in degrees_before(k):
                        degree(d, pairs)
                        degrees = d + 1
                    multiply(k, k == first_unit[n], k == last_unit[n])

        @block.vector
        def _(dve):
            def turn(k, h):
                n, r, lo, m = units[k]
                i, j = pieces(k)[h]
                if k == first_unit[n] and h == 0:
                    raw_here(dve, n)
                old = before_in_buffer(k)
                if old is not None:
                    dve.wait_ge(high_ok, old + 1)
                    dve.wait_ge(low_ok, piece_count(old, min(h if len(pieces(k)) > 1 else 1,
                                                             len(pieces(old)) - 1)))
                if k == K2:
                    dve.wait_ge(xT_ok, T // 2)
                    dve.wait_ge(degs_ok, T)
                src = raw[:, n % SLOTS, :, (lo + i) * B:(lo + j) * B].rearrange("p c (t y) -> p t c y", y=B)
                dst = turned[:, buffer(k), i * P:j * P].rearrange("p (t c x) -> p t c x", c=Q, x=B)
                dve.transpose(dst, src).then_inc(turned_ok, 3 - len(pieces(k)))

            def low(k, h):
                i, j = pieces(k)[h]
                if h == 0:
                    dve.wait_ge(high_ok, k + 1)
                    if k >= SPLITS:
                        dve.wait_ge(used, k - SPLITS + 1)
                dve.tensor_tensor(Al[:, k % SPLITS, i * P:j * P], turned[:, buffer(k), i * P:j * P],
                                  Ah[:, k % SPLITS, i * P:j * P],
                                  ALU.subtract).then_inc(low_ok, 3 - len(pieces(k)))

            def xw_out(w):
                dve.wait_ge(xw_ps, w + 1)
                dve.tensor_copy(part[:, 2 * w:2 * w + 2, :],
                                ps_y.rearrange("p (t h) -> p t h", t=2)).then_inc(xw_ok, 1)

            def take_degrees(r):
                dve.wait_ge(deg_ok, r + 1)
                dve.tensor_scalar(degs[:, r:r + 1], ps_x[:, 0:1], 1e-9, None,
                                  ALU.add).then_inc(degs_ok, 1)

            def store_part(n):
                dve.wait_ge(used, last_unit[n] + 1)
                dve.wait_ge(Yl_ok, n + 1)
                dve.scalar_tensor_tensor(out=part[:, n, :], in0=acc[:, n % 2, 0:H2], scalar=D[:, n:n + 1],
                                         in1=bias[:, :], op0=ALU.mult, op1=ALU.add).then_inc(part_ok, 1)

            def stats(j):
                dve.wait_ge(y_ok, j + 1)
                if j >= 1:
                    dve.wait_ge(aggr_ok, j)
                dve.bn_stats(st6[:, :], fin[:, j % ROWS, Y_OUT]).then_inc(stats_ok, 1)
                dve.wait_ge(stats_ok, j + 1)
                dve.bn_aggr(mv[:, j % ROWS, 0:2], st6[:, :]).then_inc(aggr_ok, 1)

            def normalise(j):
                r = loads[T - 1 + j][1]
                dve.wait_ge(rstd_ok, j + 1)
                dve.tensor_scalar(part[:, r, 0:F], fin[:, j % ROWS, Y_OUT], mv[:, j % ROWS, 0:1],
                                  mv[:, j % ROWS, 3:4], ALU.subtract, ALU.mult).then_inc(norm_ok, 1)

            def beside(k):
                for n in due(k, L_STORE):
                    if n < T - 1:
                        store_part(n)
                for j in finished(k, L_NORM):
                    normalise(j)
                for j in finished(k, L_STATS):
                    stats(j)
                if T - 1 in finished(k, L_GATE):
                    join(dve, T - 1)
                if T - 1 in finished(k, L_RELU):
                    weigh(dve, T - 1)
                if T - 1 in finished(k, L_SUM):
                    add_base(dve, T - 1)

            for w in range(LEAD // 2):
                xw_out(w)
            dve.wait_ge(const_in, 16 * 4)
            for k, (n, r, lo, m) in enumerate(units):
                p = loads[n][0]
                if p == 2:
                    turn(k, 0)
                    beside(k - 1)
                    for h in range(len(pieces(k - 1))):
                        low(k - 1, h)
                    continue
                for h in range(2):
                    if h < len(pieces(k)):
                        turn(k, h)
                    if k >= 1 and h < len(pieces(k - 1)):
                        low(k - 1, h)
                if k >= 1:
                    beside(k - 1)
                if k == (last_unit[n] - 1 if len(row_units[n]) > 3 else last_unit[n]):
                    take_degrees(r)
                if k == last_unit[n] and r >= 1:
                    for w in pair_at(r - 1):
                        xw_out(w)
            low(len(units) - 1, 0)
            for k in range(len(units) - 1, len(units) + L_NORM):
                beside(k)

        @block.scalar
        def _(act):
            junk_turn, junk_last = [0], [None, None]

            def junk_for(semaphore, count):
                h = junk_turn[0] % 2
                junk_turn[0] += 1
                if junk_last[h]:
                    act.wait_ge(*junk_last[h])
                junk_last[h] = (semaphore, count)
                return junk[:, h, :]

            sums_made = [0]

            def high(k):
                m = units[k][3]
                act.wait_ge(turned_ok, 2 * (k + 1))
                if k >= SPLITS:
                    act.wait_ge(used, k - SPLITS + 1)
                act.activation(Ah[:, k % SPLITS, 0:m * P], turned[:, buffer(k), 0:m * P],
                               ACT.Copy).then_inc(high_ok, 1)

            def row_sum(r, c):
                raw_here(act, r)
                sums_made[0] += 1
                act.activation(junk_for(rs_act, sums_made[0]), raw[:, r % SLOTS, c, :], ACT.Copy,
                               accum_out=rs[:, r, c:c + 1]).then_inc(rs_act, 1)

            def xT_out(w):
                act.wait_ge(xT_ps, w + 1)
                if w >= 1:
                    act.wait_ge(xw_ps, w)
                act.activation(xT[:, :], ps_x, ACT.Copy).then_inc(xT_ok, 1)

            def evacuate(j):
                n = T - 1 + j
                r = loads[n][1]
                act.wait_ge(used, last_unit[n] + 1)
                act.wait_ge(D_ok, r + 1)
                if j >= ROWS:
                    act.wait_ge(norm_ok, j - ROWS + 1)
                act.activation(fin[:, j % ROWS, H_ALL], acc[:, n % 2, 0:H2], ACT.Copy,
                               scale=D[:, r:r + 1]).then_inc(sums_ok, 1)

            def relu(j):
                act.wait_ge(h_ok, j + 1)
                act.activation(fin[:, j % ROWS, H_ALL], fin[:, j % ROWS, H_ALL], ACT.Relu).then_inc(relu_ok, 1)

            def gate(j):
                act.wait_ge(hw_ok, j + 1)
                act.activation(junk_for(logit_ok, j + 1)[:, 0:H2], fin[:, j % ROWS, H_ALL], ACT.Copy,
                               accum_out=lg[:, j % ROWS, 0:1]).then_inc(logit_ok, 1)
                act.wait_ge(logit_ok, j + 1)
                act.activation(lg[:, j % ROWS, 1:2], lg[:, j % ROWS, 0:1], ACT.Sigmoid,
                               bias=batt[:, :]).then_inc(gate_ok, 1)

            def beside(k):
                for j in finished(k, L_GATE):
                    gate(j)
                for j in finished(k, L_RELU):
                    relu(j)
                for j in finished(k, L_SUM):
                    evacuate(j)

            load_raw(act, 0, ACT_QUADRANTS)
            load_raw(act, 1, ACT_QUADRANTS)
            for c in range(Q):
                row_sum(0, c)
            load_raw(act, 2, ACT_QUADRANTS)
            for w in range(LEAD // 2):
                xT_out(w)
            for c in range(Q):
                row_sum(1, c)
            act.wait_ge(const_in, 16 * 4)
            for k, (n, r, lo, m) in enumerate(units):
                p = loads[n][0]
                high(k)
                for d, c in sums_after(k):
                    row_sum(d, c)
                if p == 1 and k == last_unit[n]:
                    for w in pair_at(r):
                        xT_out(w)
                if k == last_unit[n] and n + SLOTS < len(loads):
                    raw_free(act, n + SLOTS)
                    load_raw(act, n + SLOTS, ACT_QUADRANTS)
                beside(k)
            for k in range(len(units), len(units) + L_NORM):
                beside(k)

        @block.gpsimd
        def _(pool):
            def degree_weights(r):
                pool.wait_ge(rs_act, Q * (r + 1))
                if r >= 1:
                    pool.wait_ge(deg_ok, r)
                pool.tensor_tensor(degw[:, :].rearrange("p (c x) -> p c x", c=Q), same_v,
                                   rs[:, r, :].unsqueeze(2).to_broadcast([P, Q, B]),
                                   ALU.mult).then_inc(degw_ok, 1)

            def root(r):
                pool.wait_ge(degs_ok, r + 1)
                pool.tensor_tensor(D[:, r:r + 1], degs[:, r:r + 1], mhalf[:, :],
                                   ALU.pow).then_inc(D_ok, 1)

            def split_y(r):
                pool.wait_ge(xw_ok, r // 2 + 1)
                pool.wait_ge(D_ok, r + 1)
                d = D[:, r:r + 1].to_broadcast([P, H2])
                pool.tensor_tensor(Y[:, r, 0:H2], part[:, r, :], d, ALU.mult).then_inc(Yh_ok, 1)
                pool.wait_ge(Yh_ok, r + 1)
                pool.tensor_tensor(part[:, r, :], part[:, r, :], d, ALU.mult).then_inc(whole_ok, 1)
                pool.wait_ge(whole_ok, r + 1)
                pool.tensor_tensor(Y[:, r, H2:2 * H2], part[:, r, :], Y[:, r, 0:H2],
                                   ALU.subtract).then_inc(Yl_ok, 1)

            def deviation(j):
                pool.wait_ge(aggr_ok, j + 1)
                pool.tensor_tensor(mv[:, j % ROWS, 2:3], mv[:, j % ROWS, 1:2], epsc[:, :],
                                   ALU.add).then_inc(vare_ok, 1)
                pool.wait_ge(vare_ok, j + 1)
                pool.tensor_tensor(mv[:, j % ROWS, 3:4], mv[:, j % ROWS, 2:3], mhalf[:, :],
                                   ALU.pow).then_inc(rstd_ok, 1)

            same_v = same_x[:, :].rearrange("p (g d) -> p g d", g=Q)
            pool.memset(ident[:, :], 0.0).then_inc(pool_step, 1)
            pool.memset(same_x[:, :], 0.0).then_inc(pool_step, 1)
            pool.memset(ones[:, :], 1.0).then_inc(pool_step, 1)
            pool.memset(mhalf[:, :], -0.5).then_inc(pool_step, 1)
            pool.memset(epsc[:, :], 1e-5).then_inc(pool_step, 1)
            pool.wait_ge(pool_step, 5)
            pool.affine_select(out=ident[:, :], in_=ident[:, :], compare_op=ALU.not_equal, fill=1.0,
                               base=0, pattern=[[-1, P]], channel_multiplier=1).then_inc(pool_const, 1)
            for g in range(Q):
                pool.affine_select(out=same_v, in_=same_v, compare_op=ALU.not_equal, fill=1.0,
                                   base=-B * g, pattern=[[0, Q], [-1, B]],
                                   channel_multiplier=1).then_inc(pool_step, 1)
                pool.wait_ge(pool_step, 6 + g)

            for r in range(T):
                degree_weights(r)
                root(r)
                split_y(r)
            pool.wait_ge(const_in, 16 * 4)
            pool.wait_ge(Yl_ok, T)
            pool.tensor_copy(part[:, T - 1, :], bias[:, :]).then_inc(base_ok, 1)
            for k in range(last_unit[T - 1], len(units) + L_NORM):
                for j in finished(k, L_STATS):
                    deviation(j)
                for j in finished(k, L_GATE):
                    if j < T - 1:
                        join(pool, j)
                for j in finished(k, L_RELU):
                    if j < T - 1:
                        weigh(pool, j)
                for j in finished(k, L_SUM):
                    if j < T - 1:
                        add_base(pool, j)


_INS = ["x", "adj", "L0_gnn_spatial_x", "L0_gnn_W_f", "L0_gnn_b_f", "L0_gnn_W_s", "L0_gnn_b_s",
        "L0_gnn_W_att", "L0_gnn_b_att"]


def kernel(**inputs):
    import numpy as np
    import concourse.bacc as bacc
    from concourse.bass_utils import run_bass_kernel_spmd

    nc = bacc.Bacc("TRN2", target_bir_lowering=False, num_devices=1)
    arrays, args = {}, []
    for name in _INS:
        a = np.ascontiguousarray(inputs[name])
        arrays[f"in_{name}"] = a
        args.append(nc.dram_tensor(f"in_{name}", a.shape, F32, kind="ExternalInput").ap())
    args.append(nc.dram_tensor("out", arrays["in_x"].shape, F32, kind="ExternalOutput").ap())
    build(nc, *args)
    return run_bass_kernel_spmd(nc, [arrays], core_ids=[0]).results[0]["out"]
```
